# Optimizing a Trainium2 kernel written in Bass

```python
import numpy as np
import jax
import jax.numpy as jnp

def _softmax(x, axis=-1):
    return jax.nn.softmax(x, axis=axis)

def _gelu(x):
    return jax.nn.gelu(x, approximate=True)

def _silu(x):
    return jax.nn.silu(x)

def _sigmoid(x):
    return jax.nn.sigmoid(x)

def _layernorm(x, axis=-1, eps=1e-05):
    m = jnp.mean(x, axis=axis, keepdims=True)
    v = jnp.var(x, axis=axis, keepdims=True)
    return (x - m) / jnp.sqrt(v + eps)

def _scatter_add(tgt, idx, src, axis=0):
    return tgt.at[idx].add(src)

def _segment_sum(src, seg, n):
    return jax.ops.segment_sum(src, seg, n)
kernel_name = 'mk_xattn_seq_d2_seqx_r4_d09899'

def setup_inputs(seed: int=0):
    np.random.seed(seed)
    _w = jnp.asarray

    def _rec_inputs():
        import jax
        import jax.numpy as jnp
        _rk = jax.random.key(seed)
        x = -0.0005146 + 1 * jax.random.normal(jax.random.fold_in(_rk, 1), (4, 512, 512), jnp.float32)
        _lenS = 512 - jax.random.randint(jax.random.fold_in(_rk, 7), (4,), 0, max(1, 512 // 4) + 1, jnp.int32)
        _lenS2 = 1601 - jax.random.randint(jax.random.fold_in(_rk, 8), (4,), 0, max(1, 1601 // 4) + 1, jnp.int32)
        _ctx_2048P = jax.random.normal(jax.random.fold_in(_rk, 11), (4, 16, 512), jnp.float32)
        _ctx_2048c = jax.random.dirichlet(jax.random.fold_in(_rk, 511), 0.3 * jnp.ones((16,), jnp.float32), (4, 1601))
        _ctx_2048t = jnp.einsum('bsk,bkd->bsd', _ctx_2048c, _ctx_2048P)
        _ctx_2048t = _ctx_2048t * jax.lax.rsqrt(jnp.mean(jnp.square(_ctx_2048t)) + 1e-12) * 0.953939
        ctx_2048 = -0.000392918 + 0.999932 * (_ctx_2048t + 0.3 * jax.random.normal(jax.random.fold_in(_rk, 611), (4, 1601, 512), jnp.float32))
        _validS = jnp.arange(512)[None, :] < _lenS[:, None]
        _validS2 = jnp.arange(1601)[None, :] < _lenS2[:, None]
        _causal = jnp.tril(jnp.ones((512, 512), dtype=bool))
        mask_BxS2_ik0 = jnp.where(jnp.broadcast_to(_validS2[:, :], (4, 1601)), 0, 1).astype(jnp.int32)
        mask_Bx1xSxS2_ff0 = jnp.where(jnp.ones((4, 1, 512, 1601), dtype=bool), 0.0, -1000000000.0).astype(jnp.float32)
        return (x, ctx_2048, mask_BxS2_ik0, mask_Bx1xSxS2_ff0)
    x, ctx_2048, mask_BxS2_ik0, mask_Bx1xSxS2_ff0 = _rec_inputs()

    def _L0_xattn_setup():
        import jax, jax.numpy as jnp
        import numpy as np
        B, P, K, H, NH = (4, 512, 64, 512, 16)
        DH = H // NH
        EPS = 1e-06

        def rmsnorm(x, w):
            var = jnp.mean(jnp.square(x), axis=-1, keepdims=True)
            return x * jax.lax.rsqrt(var + EPS) * w
        key = jax.random.key(seed)
        ks = jax.random.split(key, 12)
        s = 0.02
        return {'x': jax.random.normal(ks[0], (B, P, H), jnp.float32), 'latents': jax.random.normal(ks[1], (B, K, H), jnp.float32), 'attention_mask': jax.random.randint(ks[2], (B, P), 0, 2, jnp.int32), 'q_w': s * jax.random.normal(ks[3], (H, H), jnp.float32), 'q_b': jnp.zeros((H,), jnp.float32), 'kv_w': s * jax.random.normal(ks[4], (H, 2 * H), jnp.float32), 'kv_b': jnp.zeros((2 * H,), jnp.float32), 'out_w': s * jax.random.normal(ks[5], (H, H), jnp.float32), 'out_b': jnp.zeros((H,), jnp.float32), 'postnorm_w': jnp.ones((H,), jnp.float32), 'mlp_w1': s * jax.random.normal(ks[6], (H, 4 * H), jnp.float32), 'mlp_b1': jnp.zeros((4 * H,), jnp.float32), 'mlp_w2': s * jax.random.normal(ks[7], (4 * H, H), jnp.float32), 'mlp_b2': jnp.zeros((H,), jnp.float32)}
    _L0_xattn_all = _L0_xattn_setup()
    _L0_xattn_in = {k: v for k, v in _L0_xattn_all.items() if k in ('q_w', 'q_b', 'kv_w', 'kv_b', 'out_w', 'out_b', 'postnorm_w', 'mlp_w1', 'mlp_b1', 'mlp_w2', 'mlp_b2')}
    del _L0_xattn_all

    def _L1_xattn_setup():
        import jax, jax.numpy as jnp
        import numpy as np
        H = 512
        NH = 32
        KVH = 8
        HD = H // NH
        GROUPS = NH // KVH
        EPS = 1e-06
        B, L, S = (4, 256, 256)

        def _gqa_forward(hidden_state, encoder_hidden_state, encoder_attention_mask, Wq, bq, Wk, bk, Wv, bv, Wo, bo, gamma, beta):
            b, l, _ = hidden_state.shape
            s = encoder_hidden_state.shape[1]
            q = hidden_state @ Wq + bq
            k = encoder_hidden_state @ Wk + bk
            v = encoder_hidden_state @ Wv + bv
            q = q.reshape(b, l, KVH, GROUPS, HD).transpose(0, 2, 3, 1, 4)
            k = k.reshape(b, s, KVH, HD).transpose(0, 2, 1, 3)
            v = v.reshape(b, s, KVH, HD).transpose(0, 2, 1, 3)
            scale = 1.0 / jnp.sqrt(jnp.asarray(HD, q.dtype))
            scores = jnp.einsum('bkgld,bksd->bkgls', q, k) * scale
            scores = scores + encoder_attention_mask[:, :, None, :, :]
            attn = jax.nn.softmax(scores, axis=-1)
            out = jnp.einsum('bkgls,bksd->bkgld', attn, v)
            out = out.transpose(0, 3, 1, 2, 4).reshape(b, l, H)
            out = out @ Wo + bo
            x = out + hidden_state
            mu = jnp.mean(x, axis=-1, keepdims=True)
            var = jnp.var(x, axis=-1, keepdims=True)
            return (x - mu) * jax.lax.rsqrt(var + EPS) * gamma + beta
        key = jax.random.key(seed)
        ks = jax.random.split(key, 12)
        sd = 0.02
        return {'hidden_state': jax.random.normal(ks[0], (B, L, H), jnp.float32), 'encoder_hidden_state': jax.random.normal(ks[1], (B, S, H), jnp.float32), 'encoder_attention_mask': jnp.zeros((B, 1, L, S), jnp.float32), 'Wq': jax.random.normal(ks[2], (H, H), jnp.float32) * sd, 'bq': jnp.zeros((H,), jnp.float32), 'Wk': jax.random.normal(ks[3], (H, KVH * HD), jnp.float32) * sd, 'bk': jnp.zeros((KVH * HD,), jnp.float32), 'Wv': jax.random.normal(ks[4], (H, KVH * HD), jnp.float32) * sd, 'bv': jnp.zeros((KVH * HD,), jnp.float32), 'Wo': jax.random.normal(ks[5], (H, H), jnp.float32) * sd, 'bo': jnp.zeros((H,), jnp.float32), 'gamma': jnp.ones((H,), jnp.float32), 'beta': jnp.zeros((H,), jnp.float32)}
    _L1_xattn_all = _L1_xattn_setup()
    _L1_xattn_in = {k: v for k, v in _L1_xattn_all.items() if k in ('Wq', 'bq', 'Wk', 'bk', 'Wv', 'bv', 'Wo', 'bo', 'gamma', 'beta')}
    del _L1_xattn_all
    return {'x': x, 'ctx_2048': ctx_2048, 'mask_BxS2_ik0': mask_BxS2_ik0, 'mask_Bx1xSxS2_ff0': mask_Bx1xSxS2_ff0, 'L0_xattn_q_w': _L0_xattn_in['q_w'], 'L0_xattn_q_b': _L0_xattn_in['q_b'], 'L0_xattn_kv_w': _L0_xattn_in['kv_w'], 'L0_xattn_kv_b': _L0_xattn_in['kv_b'], 'L0_xattn_out_w': _L0_xattn_in['out_w'], 'L0_xattn_out_b': _L0_xattn_in['out_b'], 'L0_xattn_postnorm_w': _L0_xattn_in['postnorm_w'], 'L0_xattn_mlp_w1': _L0_xattn_in['mlp_w1'], 'L0_xattn_mlp_b1': _L0_xattn_in['mlp_b1'], 'L0_xattn_mlp_w2': _L0_xattn_in['mlp_w2'], 'L0_xattn_mlp_b2': _L0_xattn_in['mlp_b2'], 'L1_xattn_Wq': _L1_xattn_in['Wq'], 'L1_xattn_bq': _L1_xattn_in['bq'], 'L1_xattn_Wk': _L1_xattn_in['Wk'], 'L1_xattn_bk': _L1_xattn_in['bk'], 'L1_xattn_Wv': _L1_xattn_in['Wv'], 'L1_xattn_bv': _L1_xattn_in['bv'], 'L1_xattn_Wo': _L1_xattn_in['Wo'], 'L1_xattn_bo': _L1_xattn_in['bo'], 'L1_xattn_gamma': _L1_xattn_in['gamma'], 'L1_xattn_beta': _L1_xattn_in['beta']}

def reference(x, ctx_2048, mask_BxS2_ik0, mask_Bx1xSxS2_ff0, L0_xattn_q_w, L0_xattn_q_b, L0_xattn_kv_w, L0_xattn_kv_b, L0_xattn_out_w, L0_xattn_out_b, L0_xattn_postnorm_w, L0_xattn_mlp_w1, L0_xattn_mlp_b1, L0_xattn_mlp_w2, L0_xattn_mlp_b2, L1_xattn_Wq, L1_xattn_bq, L1_xattn_Wk, L1_xattn_bk, L1_xattn_Wv, L1_xattn_bv, L1_xattn_Wo, L1_xattn_bo, L1_xattn_gamma, L1_xattn_beta):
    import jax
    import jax.numpy as jnp

    def _L0_xattn_ref(x, latents, attention_mask, q_w, q_b, kv_w, kv_b, out_w, out_b, postnorm_w, mlp_w1, mlp_b1, mlp_w2, mlp_b2):
        import jax, jax.numpy as jnp
        import numpy as np
        B, P, K, H, NH = (4, 512, 64, 512, 16)
        DH = H // NH
        EPS = 1e-06

        def rmsnorm(x, w):
            var = jnp.mean(jnp.square(x), axis=-1, keepdims=True)
            return x * jax.lax.rsqrt(var + EPS) * w
        b, p, _ = x.shape
        k_len = latents.shape[1]
        residual = latents
        h = jnp.concatenate([x, latents], axis=1)
        q = (latents @ q_w + q_b).reshape(b, k_len, NH, DH)
        kv = (h @ kv_w + kv_b).reshape(b, p + k_len, NH, DH, 2)
        kmat, v = (kv[..., 0], kv[..., 1])
        attn = jnp.einsum('bkhd,bnhd->bhkn', q, kmat) / DH
        full_mask = jnp.concatenate([attention_mask.astype(bool), jnp.ones((b, k_len), bool)], axis=-1)
        attn = jnp.where(full_mask[:, None, None, :], attn, -jnp.inf)
        attn = jax.nn.softmax(attn.astype(jnp.float32), axis=-1).astype(q.dtype)
        attn_out = jnp.einsum('bhkn,bnhd->bkhd', attn, v).reshape(b, k_len, H)
        attn_out = attn_out @ out_w + out_b + residual
        out = rmsnorm(attn_out, postnorm_w)
        out = jax.nn.gelu(out @ mlp_w1 + mlp_b1) @ mlp_w2 + mlp_b2
        return out + residual

    def _L1_xattn_ref(hidden_state, encoder_hidden_state, encoder_attention_mask, Wq, bq, Wk, bk, Wv, bv, Wo, bo, gamma, beta):
        import jax, jax.numpy as jnp
        import numpy as np
        H = 512
        NH = 32
        KVH = 8
        HD = H // NH
        GROUPS = NH // KVH
        EPS = 1e-06
        B, L, S = (4, 256, 256)

        def _gqa_forward(hidden_state, encoder_hidden_state, encoder_attention_mask, Wq, bq, Wk, bk, Wv, bv, Wo, bo, gamma, beta):
            b, l, _ = hidden_state.shape
            s = encoder_hidden_state.shape[1]
            q = hidden_state @ Wq + bq
            k = encoder_hidden_state @ Wk + bk
            v = encoder_hidden_state @ Wv + bv
            q = q.reshape(b, l, KVH, GROUPS, HD).transpose(0, 2, 3, 1, 4)
            k = k.reshape(b, s, KVH, HD).transpose(0, 2, 1, 3)
            v = v.reshape(b, s, KVH, HD).transpose(0, 2, 1, 3)
            scale = 1.0 / jnp.sqrt(jnp.asarray(HD, q.dtype))
            scores = jnp.einsum('bkgld,bksd->bkgls', q, k) * scale
            scores = scores + encoder_attention_mask[:, :, None, :, :]
            attn = jax.nn.softmax(scores, axis=-1)
            out = jnp.einsum('bkgls,bksd->bkgld', attn, v)
            out = out.transpose(0, 3, 1, 2, 4).reshape(b, l, H)
            out = out @ Wo + bo
            x = out + hidden_state
            mu = jnp.mean(x, axis=-1, keepdims=True)
            var = jnp.var(x, axis=-1, keepdims=True)
            return (x - mu) * jax.lax.rsqrt(var + EPS) * gamma + beta
        return _gqa_forward(hidden_state, encoder_hidden_state, encoder_attention_mask, Wq, bq, Wk, bk, Wv, bv, Wo, bo, gamma, beta)
    x = _L0_xattn_ref(ctx_2048, x, mask_BxS2_ik0, L0_xattn_q_w, L0_xattn_q_b, L0_xattn_kv_w, L0_xattn_kv_b, L0_xattn_out_w, L0_xattn_out_b, L0_xattn_postnorm_w, L0_xattn_mlp_w1, L0_xattn_mlp_b1, L0_xattn_mlp_w2, L0_xattn_mlp_b2)
    x = _L1_xattn_ref(x, ctx_2048, mask_Bx1xSxS2_ff0, L1_xattn_Wq, L1_xattn_bq, L1_xattn_Wk, L1_xattn_bk, L1_xattn_Wv, L1_xattn_bv, L1_xattn_Wo, L1_xattn_bo, L1_xattn_gamma, L1_xattn_beta)
    return x

_drawn_inputs = setup_inputs


def setup_inputs(seed=0):
    import zlib

    import numpy as np

    out = dict(_drawn_inputs(seed))
    spreads = {'L0_xattn_q_b': (0.0, 0.8),
     'L0_xattn_kv_b': (0.0, 0.774),
     'L0_xattn_out_b': (0.0, 0.342),
     'L0_xattn_postnorm_w': (1.0, 0.2),
     'L0_xattn_mlp_b1': (0.0, 0.1),
     'L0_xattn_mlp_b2': (0.0, 0.1),
     'L1_xattn_bq': (0.0, 0.8),
     'L1_xattn_bk': (0.0, 0.8),
     'L1_xattn_bv': (0.0, 0.1),
     'L1_xattn_bo': (0.0, 0.1),
     'L1_xattn_gamma': (1.0, 0.2),
     'L1_xattn_beta': (0.0, 0.1)}
    factors = {'L0_xattn_q_w': 8.0,
     'L0_xattn_kv_w': 5.547,
     'L0_xattn_out_w': 4.147,
     'L1_xattn_Wq': 7.866,
     'L1_xattn_Wk': 7.733}
    for name, (base, spread) in spreads.items():
        noise = np.random.default_rng([zlib.crc32(name.encode()), seed]).standard_normal(out[name].shape)
        drawn = base * np.exp(spread * noise) if base else spread * noise
        out[name] = jnp.asarray(drawn.astype(out[name].dtype))
    for name, factor in factors.items():
        out[name] = (out[name] * factor).astype(out[name].dtype)
    return out
```

```python
from contextlib import ExitStack

import concourse.bass as bass
from concourse import mybir
from concourse.alu_op_type import AluOpType as ALU

F32 = mybir.dt.float32
F32R = mybir.dt.float32r
I32 = mybir.dt.int32
ACT = mybir.ActivationFunctionType
AX = mybir.AxisListType

P = 128
B = 4
D = 512
KO = D // P
L = 512
QT = L // P
S = 1601
FF = 2048
NF = FF // P
FIRST_CHUNKS = (4, 0, 1, 2, 3)
BIG = 1e30
SPLIT = ((0, 0), (0, 1), (1, 0))
EPS = 1e-6

H0, D0 = 16, 32
N0 = S + L
T0 = -(-N0 // P)
PAIRS0 = -(-T0 // 2)
CH0 = [0, 424, 848, 1272, 1696, N0 + 1]
PR0 = [0, 400, 800, 1200, S, N0]
H1, D1, KV1 = 32, 16, 8
N1 = S
T1 = -(-N1 // P)
PAIRS1 = -(-T1 // 2)
CH1 = [0, 400, 800, 1200, N1 + 1]
GQ = H1 // KV1
NR = 3
SLOTS = 4
NPT0, NPT1 = 4, 5
DVE_SUMS = H0 - 2
POOL_PAIRS = (0, 1, 3, 5)


def rows(tile, n):
    return min(P, n - tile * P)


def order(plan, *kinds):
    out, n = {}, 0
    for item in plan:
        if item[0] in kinds:
            n += 1
            out[item] = n
    return out


def attention_plan(heads, chunks, pairs, per_group, prologue, extra, exp_lag, pv_lag, sums):
    plan = list(prologue)
    steps = [(h, p) for h in range(heads) for p in range(pairs)]
    queue, later = [], {}
    for i in range(len(steps) + pv_lag + 5):
        if i < len(steps):
            h, p = steps[i]
            if p == 0 and h + 2 < heads:
                queue = [("A", h + 2, qt, c) for qt in range(QT) for c in range(chunks)] + [("N", h + 2)]
            plan.append(("B", h, p))
            share = -(-len(queue) // (pairs - p))
            plan += queue[:share // 2]
            plan += extra.get((h, p), [])
        if 0 <= i - exp_lag < len(steps):
            plan.append(("P", *steps[i - exp_lag]))
        if 0 <= i - pv_lag < len(steps):
            h, p = steps[i - pv_lag]
            plan.append(("W", h, p))
            if p == pairs - 1:
                plan.append(("E", h))
                if sums:
                    later.setdefault(i + 2, []).append(("S", h))
                if h % per_group == per_group - 1:
                    later.setdefault(i + 2, []).append(("Y", h // per_group))
                    later.setdefault(i + 4, []).append(("X", h // per_group))
        if i < len(steps):
            plan += queue[share // 2:share]
            queue = queue[share:]
        plan += later.pop(i, [])
        if i < len(steps) and steps[i][1] == pairs // 2 and steps[i][0] + 1 < heads:
            plan.append(("M", steps[i][0] + 1))
    assert not later
    out, open_steps = [], []
    for item in plan:
        out.append(item)
        if item[0] in ("A", "B") and open_steps:
            out.append(open_steps.pop(0))
        elif item[0] == "N":
            assert not open_steps
            open_steps = [("H", item[1]), ("L", item[1])]
    assert not open_steps
    return out


def plan_layer0():
    first = [("Q", 0)] + [("K", 0, c) for c in FIRST_CHUNKS]
    a = [("A", h, qt, c) for h in (0, 1) for qt in range(QT) for c in range(5)]
    a.insert(20, ("N", 0))
    a.append(("N", 1))
    for t in range(T0):
        first.append(("V", t))
        share = -(-len(a) // (T0 - t))
        if t >= 4:
            first += a[:share]
            a = a[share:]
    first.append(("M", 0))
    extra = {}
    for g in range(1, H0 // 4):
        pieces = [("Q", g)] + [("K", g, c) for c in range(5)]
        for i, x in enumerate(pieces):
            extra[(4 * (g - 1) + i // 3, 1 + 2 * (i % 3))] = [x]
    return attention_plan(H0, 5, PAIRS0, 4, first, extra, 0, 2, True)


def plan_layer1():
    a = []
    for h in (0, 1):
        a += [("A", h, qt, c) for qt in range(QT) for c in range(4)] + [("N", h)]
    plan = attention_plan(H1, 4, PAIRS1, 8, a + [("M", 0)], {}, 2, 3, False)
    plan.insert(plan.index(("W", H1 - 1, PAIRS1 - 2)), ("O",))
    return plan


def narrow_weights(tile):
    return tile[:, :, 0:P], tile[:, :, P:2 * P]


def layer0_attention(nc, ctx, ios, b, keep, sem):
    plan = plan_layer0()
    attnT, ident, sel = keep["attnT"], keep["identR"], keep["sel"]

    def sb(name, shape, dt=F32):
        return ctx.enter_context(nc.sbuf_tensor("l0_" + name, shape, dt))

    def ps(name, shape):
        return ctx.enter_context(nc.psum_tensor("l0_" + name, shape, F32))

    hT = keep["hT"]
    wq, wk, wv = keep["tile_a"], keep["tile_b"], keep["tile_c"]
    bq, bqs, bk = (sb(n, [P, KO]) for n in ("bq", "bqs", "bk"))
    bv = sb("bv", [P, D])
    tcol = sb("tcol", [P, 4])
    qlast = sb("qlast", [P, L], F32R)
    kst = sb("kst", [P, SLOTS, N0 + 1], F32R)
    qst = sb("qst", [P, SLOTS, L], F32R)
    khl = sb("khl", [P, 2, N0], F32R)
    qhl = sb("qhl", [P, 2, L], F32R)
    val = sb("val", [P, 2, 512])
    V = sb("V", [P, T0, D])
    ones = sb("ones", [P, D0])
    mask = V[:, 12:16, :].bitcast(I32).rearrange("p a n -> p (a n)")[:, 0:S]
    pen = V[:, 6:11, :].rearrange("p a n -> p (a n)")[:, 0:N0 + 1]
    pt = sb("pt", [P, NPT0, 1024])
    psum = sb("psum", [P, 2, 1024])
    osb = sb("osb", [P, 4, L])
    rsum = sb("rsum", [P, L])
    acc = sb("acc", [P, 2, QT, 5])
    nmax = sb("nmax", [P, 2, QT])
    mz = sb("mz", [P, 2, QT, 98], F32R)
    psR = ps("psR", [P, NR, 512])
    psB, psO = ps("psB", [P, 4, 512]), ps("psO", [P, 512])

    s_wq0, s_wk0, s_w, s_wv, s_c, s_x = (sem("l0_" + n) for n in ("wq_first_in", "wk_first_in", "w_in", "wv_in", "const_in", "x_in"))
    s_wo_mid, s_wkv_mid, s_x_mid = sem("mid_wo_in"), sem("mid_wkv1_in"), sem("mid_x_in")
    s_h = [sem(f"l0_ctx_in{i}") for i in range(4)]
    s_stack = [sem(f"l0_stack_in{i}") for i in range(SLOTS)]
    s_pen, s_last, s_pad, s_bqs, s_ones = (sem("l0_" + n) for n in ("penalty", "last_rows", "pad", "bqs", "ones"))
    s_m = sem("l0_m_full")
    s_val, s_split = sem("l0_val"), sem("l0_split")
    s_v, s_vout = sem("l0_v_full"), sem("l0_v_done")
    s_a, s_red = sem("l0_a_full"), sem("l0_a_reduced")
    s_nm, s_mh, s_ml = sem("l0_nmax"), sem("l0_max_hi"), sem("l0_max_hilo")
    s_b, s_exp, s_pv = sem("l0_b_full"), sem("l0_exp"), sem("l0_pv")
    s_osb = sem("l0_osb")
    s_rs, s_att = sem("l0_rsum"), sem("l0_att")
    s_rows, s_zero = sem("l0_max_rows"), sem("l0_zeros")
    s_acc, s_sum = sem("l0_exp_summed"), sem("l0_sums")

    ring = order(plan, "Q", "K", "A", "M", "S", "X")
    in_ring = [x for x in plan if x in ring]
    m_uses = order(plan, "Q", "K", "M", "S", "X")
    kq = order(plan, "Q", "K")
    va = order(plan, "V")
    aa = order(plan, "A")
    bb = order(plan, "B")
    chunk_in = [s_h[0], s_h[1], s_h[2], s_h[3], s_x]

    x_mid, (wk1, wv1) = keep["tile_a"], narrow_weights(keep["tile_b"])

    block = ctx.enter_context(nc.Block())

    @block.sync
    def _(sp):
        def copy(out, part):
            return sp.dma_start(out.bitcast(F32), part.bitcast(F32))

        sp.dma_start(wq[:, :, 0:P], ios["wq0"][:, :, 0:P]).then_inc(s_wq0, 16)
        sp.dma_start(hT[:, :, S:N0], ios["xT"][b]).then_inc(s_x, 16)
        sp.dma_start(wk[:, :, 0:P], ios["wk0"][:, :, 0:P]).then_inc(s_wk0, 16)
        for i in range(4):
            sp.dma_start(hT[:, :, PR0[i]:PR0[i + 1]], ios["ctxT"][b, :, :, PR0[i]:PR0[i + 1]]).then_inc(s_h[i], 16)
        sp.dma_start(wv[:, :, :], ios["wv0"]).then_inc(s_wv, 16)
        sp.dma_start(wq[:, :, P:D], ios["wq0"][:, :, P:D]).then_inc(s_w, 16)
        sp.dma_start(wk[:, :, P:D], ios["wk0"][:, :, P:D]).then_inc(s_w, 16)
        for h in range(H0):
            g, j, s = h // 4, h % 4, h % SLOTS
            sp.wait_ge(s_split, 6 * (g + 1))
            if h == 0:
                sp.wait_ge(s_last, 5)
            if h >= SLOTS:
                sp.wait_ge(s_b, bb[("B", h - SLOTS, PAIRS0 - 1)])
            q = slice(32 * j, 32 * j + 32)
            for r, part in enumerate((0, 0, 1)):
                copy(qst[32 * r:32 * r + 32, s, :], qhl[q, part, :]).then_inc(s_stack[s], 16)
            copy(qst[96:128, s, :], qlast[96:128, :]).then_inc(s_stack[s], 16)
            for r, part in enumerate((0, 1, 0)):
                copy(kst[32 * r:32 * r + 32, s, 0:N0], khl[q, part, :]).then_inc(s_stack[s], 16)
        sp.dma_start(x_mid[:, :, :], ios["x"][b]).then_inc(s_x_mid, 16)
        sp.dma_start(wk1[:, :, :], ios["wk1"]).then_inc(s_wkv_mid, 16)
        sp.dma_start(wv1[:, :, :], ios["wv1"]).then_inc(s_wkv_mid, 16)
        sp.wait_ge(s_v, T0)
        sp.dma_start(wv[:, :, :], ios["wo0"]).then_inc(s_wo_mid, 16)

    @block.gpsimd
    def _(pool):
        for s in range(SLOTS):
            pool.memset(kst[0:96, s, N0:N0 + 1].bitcast(F32), 0.0).then_inc(s_pad, 1)
        pool.memset(mz[:, :, :, 0:96].bitcast(F32), 0.0).then_inc(s_zero, 1)
        for item in plan:
            if item[0] in "QK":
                n, g = kq[item], item[1]
                dst, w = (qhl, slice(0, L)) if item[0] == "Q" else (khl, slice(PR0[item[2]], PR0[item[2] + 1]))
                pool.wait_ge(s_val, n)
                pool.tensor_tensor(dst[:, 1, w], val[:, n % 2, 0:w.stop - w.start], dst[:, 0, w].bitcast(F32),
                                   ALU.subtract).then_inc(s_split, 1)
            elif item[0] == "P":
                _, h, p = item
                n, a = bb[("B", h, p)], h % 2
                if p == 0 or h >= DVE_SUMS:
                    continue
                pool.wait_ge(s_exp, n)
                if p == 1:
                    if h >= 2:
                        pool.wait_ge(s_m, m_uses[("S", h - 2)])
                    pool.tensor_tensor(psum[:, a, :], pt[:, (n - 1) % NPT0, :], pt[:, n % NPT0, :], ALU.add)\
                        .then_inc(s_acc, 1)
                else:
                    pool.wait_ge(s_acc, 8 * h + p - 1)
                    r, w = (P, 1024) if p < PAIRS0 - 1 else (rows(T0 - 1, N0), 512)
                    pool.tensor_tensor(psum[0:r, a, 0:w], psum[0:r, a, 0:w], pt[0:r, n % NPT0, 0:w], ALU.add)\
                        .then_inc(s_acc, 1)

    @block.scalar
    def _(act):
        act.dma_start(bq[:, :], ios["bq0"]).then_inc(s_c, 16)
        act.dma_start(bk[:, :], ios["bk0"]).then_inc(s_c, 16)
        act.dma_start(bv[:, :], ios["bv0"].partition_broadcast(P)).then_inc(s_c, 16)
        act.dma_start(mask[96:128, :], ios["mask"][b].partition_broadcast(32)).then_inc(s_c, 16)
        act.dma_start(tcol[96:128, :], ios["tcol"]).then_inc(s_c, 16)
        for item in plan:
            if item[0] in "QK":
                n, g, q = kq[item], item[1], item[0] == "Q"
                if n == 1:
                    act.wait_ge(s_bqs, 1)
                psM = psR[:, ring[item] % NR, :]
                act.wait_ge(s_m, m_uses[item])
                if n > 2:
                    act.wait_ge(s_split, n - 2)
                if g and q:
                    for s in range(SLOTS):
                        act.wait_ge(s_stack[s], 112 * g)
                lo = 0 if q else PR0[item[2]]
                n_w = L if q else PR0[item[2] + 1] - lo
                bias, scale = (bqs if q else bk)[:, g:g + 1], 1.0 / D0 if q else 1.0
                act.activation((qhl if q else khl)[:, 0, lo:lo + n_w], psM[:, 0:n_w], ACT.Identity, bias=bias, scale=scale)
                act.activation(val[:, n % 2, 0:n_w], psM[:, 0:n_w], ACT.Identity, bias=bias, scale=scale)\
                   .then_inc(s_val, 1)
            elif item[0] == "M":
                psM = psR[:, ring[item] % NR, :]
                act.wait_ge(s_m, m_uses[item])
                act.activation(qst[96:98, item[1] % SLOTS, :], psM[96:98, :], ACT.Copy).then_inc(s_rows, 1)
            elif item[0] == "S":
                g, j = item[1] // 4, item[1] % 4
                psM = psR[:, ring[item] % NR, :]
                act.wait_ge(s_m, m_uses[item])
                if g and j == 0:
                    act.wait_ge(s_att, g)
                act.activation(rsum[32 * j:32 * j + 32, :], psM[32 * j:32 * j + 32, :], ACT.Copy).then_inc(s_sum, 1)
            elif item[0] == "P":
                n, kt = bb[("B", *item[1:])], 2 * item[2]
                r, w = (P, 1024) if kt + 1 < T0 else (rows(kt, N0), 512)
                act.wait_ge(s_b, n)
                if n > NPT0:
                    act.wait_ge(s_pv, n - NPT0)
                    h, p = divmod(n - NPT0 - 1, PAIRS0)
                    act.wait_ge(s_acc, 8 * h + max(p, 1))
                act.activation(pt[0:r, n % NPT0, 0:w],
                               psB[0:r, 2 * (n % 2):2 * (n % 2) + 2, :].rearrange("p a n -> p (a n)")[:, 0:w],
                               ACT.Exp).then_inc(s_exp, 1)

    @block.vector
    def _(dve):
        dve.memset(ones[:, :], 1.0).then_inc(s_ones, 1)
        dve.wait_ge(s_c, 80)
        dve.tensor_scalar(bqs[:, :], bq[:, :], 1.0 / D0, None, ALU.mult).then_inc(s_bqs, 1)
        dve.tensor_scalar(pen[96:128, 0:S], mask[96:128, :], 0, -BIG, ALU.is_equal, ALU.mult).then_inc(s_pen, 1)
        dve.memset(pen[96:128, S:N0 + 1], 0.0).then_inc(s_pen, 1)
        dve.wait_ge(s_pen, 2)
        dve.tensor_scalar(qlast[96:128, :], pen[96:128, 0:L], 0.0, tcol[96:128, 2:3], ALU.mult, ALU.add).then_inc(s_last, 1)
        for s in range(SLOTS):
            dve.tensor_scalar(kst[96:128, s, :], pen[96:128, :], tcol[96:128, 0:1], tcol[96:128, 1:2],
                              ALU.mult, ALU.add).then_inc(s_last, 1)
        for item in plan:
            if item[0] == "V":
                n, t = va[item], item[1]
                r = rows(t, N0)
                dve.wait_ge(s_v, n)
                dve.tensor_tensor(V[0:r, t, :], psB[0:r, t % 4, :], bv[0:r, :], ALU.add).then_inc(s_vout, 1)
            elif item[0] == "A":
                _, h, qt, c = item
                n, w = aa[item], min(CH0[c + 1], N0) - CH0[c]
                dve.wait_ge(s_a, n)
                if h >= 2 and qt == c == 0:
                    dve.wait_ge(s_nm, h - 1)
                dve.tensor_reduce(acc[:, h % 2, qt, c:c + 1], psR[:, ring[item] % NR, 0:w], AX.X, ALU.max).then_inc(s_red, 1)
            elif item[0] == "N":
                h = item[1]
                dve.wait_ge(s_red, 20 * (h + 1))
                dve.tensor_reduce(nmax[:, h % 2, :], acc[:, h % 2, :, :], AX.X, ALU.max, negate=True).then_inc(s_nm, 1)
            elif item[0] == "H":
                h = item[1]
                dve.wait_ge(s_nm, h + 1)
                if h >= 2:
                    dve.wait_ge(s_m, m_uses[("M", h - 2)])
                dve.tensor_copy(mz[:, h % 2, :, 96], nmax[:, h % 2, :]).then_inc(s_mh, 1)
            elif item[0] == "L":
                h = item[1]
                dve.wait_ge(s_mh, h + 1)
                dve.tensor_tensor(mz[:, h % 2, :, 97], nmax[:, h % 2, :], mz[:, h % 2, :, 96].bitcast(F32),
                                  ALU.subtract).then_inc(s_ml, 1)
            elif item[0] == "W" and item[1] >= DVE_SUMS and item[2]:
                _, h, p = item
                n, a = bb[("B", h, p)], h % 2
                r, w = (P, 1024) if p < PAIRS0 - 1 else (rows(T0 - 1, N0), 512)
                dve.wait_ge(s_exp, n)
                if p == 1:
                    dve.wait_ge(s_m, m_uses[("S", h - 2)])
                    before = pt[:, (n - 1) % NPT0, :]
                else:
                    before = psum[0:r, a, 0:w]
                dve.wait_ge(s_acc, 8 * h + p - 1)
                dve.tensor_tensor(psum[0:r, a, 0:w], before, pt[0:r, n % NPT0, 0:w], ALU.add).then_inc(s_acc, 1)
            elif item[0] == "E":
                h = item[1]
                dve.wait_ge(s_pv, PAIRS0 * (h + 1))
                if h >= 4:
                    dve.wait_ge(s_m, m_uses[("X", h // 4 - 1)])
                dve.tensor_copy(osb[:, h % 4, :], psO[:, :]).then_inc(s_osb, 1)
            elif item[0] == "Y":
                dve.wait_ge(s_sum, 4 * (item[1] + 1))
                dve.reciprocal(rsum[:, :], rsum[:, :]).then_inc(s_rs, 1)
            elif item[0] == "X":
                psM = psR[:, ring[item] % NR, :]
                dve.wait_ge(s_m, m_uses[item])
                dve.wait_ge(s_rs, item[1] + 1)
                dve.tensor_tensor(attnT[:, item[1], :], psM, rsum[:, :], ALU.mult).then_inc(s_att, 1)

    @block.tensor
    def _(pe):
        for item in plan:
            k = item[0]
            if item in ring:
                psM = psR[:, ring[item] % NR, :]
                if ring[item] > NR:
                    last = in_ring[ring[item] - NR - 1]
                    pe.wait_ge({"Q": s_val, "K": s_val, "A": s_red, "M": s_rows, "S": s_sum, "X": s_att}[last[0]],
                               kq[last] if last in kq else aa[last] if last in aa else last[1] + 1)
            if k in ("Q", "K"):
                g = item[1]
                if k == "Q":
                    lo, hi, w = S, N0, wq
                    pe.wait_ge(s_x, 16)
                else:
                    lo, hi, w = PR0[item[2]], PR0[item[2] + 1], wk
                    pe.wait_ge(chunk_in[item[2]], 16)
                if g:
                    pe.wait_ge(s_w, 32)
                else:
                    pe.wait_ge(s_wq0 if k == "Q" else s_wk0, 16)
                for ko in range(KO):
                    mm = pe.matmul(psM[:, 0:hi - lo], w[:, ko, g * P:(g + 1) * P], hT[:, ko, lo:hi],
                                   start=(ko == 0), stop=(ko == KO - 1))
                mm.then_inc(s_m, 1)
            elif k == "V":
                t = item[1]
                r = rows(t, N0)
                pe.wait_ge(s_wv, 16)
                if t >= 4:
                    pe.wait_ge(s_vout, t - 3)
                for ko in range(KO):
                    mm = pe.matmul(psB[0:r, t % 4, :], hT[:, ko, t * P:t * P + r], wv[:, ko, :],
                                   start=(ko == 0), stop=(ko == KO - 1))
                mm.then_inc(s_v, 1)
            elif k == "A":
                _, h, qt, c = item
                n, s = aa[item], h % SLOTS
                if qt == c == 0:
                    pe.wait_ge(s_stack[s], 112 * (h // SLOTS + 1))
                    pe.wait_ge(s_pad, SLOTS)
                pe.matmul(psM[:, 0:CH0[c + 1] - CH0[c]], qst[:, s, qt * P:(qt + 1) * P],
                          kst[:, s, CH0[c]:CH0[c + 1]], start=True, stop=True).then_inc(s_a, 1)
            elif k == "M":
                h = item[1]
                pe.wait_ge(s_ml, h + 1)
                if h == 0:
                    pe.wait_ge(s_zero, 1)
                for qt in range(QT):
                    mm = pe.matmul(psM[0:98, qt * P:(qt + 1) * P], mz[:, h % 2, qt, :], ident[:, :],
                                   start=True, stop=True)
                mm.then_inc(s_m, 1)
            elif k == "B":
                _, h, p = item
                n, s = bb[item], h % SLOTS
                if p == 0:
                    pe.wait_ge(s_rows, h + 1)
                if n <= 2:
                    pe.wait_ge(s_vout, T0)
                else:
                    pe.wait_ge(s_exp, n - 2)
                for kt in range(2 * p, min(2 * p + 2, T0)):
                    r = rows(kt, N0)
                    mm = pe.matmul(psB[0:r, 2 * (n % 2) + kt % 2, :], kst[:, s, kt * P:kt * P + r], qst[:, s, :],
                                   start=True, stop=True)
                mm.then_inc(s_b, 1)
            elif k == "W":
                _, h, p = item
                n = bb[("B", h, p)]
                pe.wait_ge(s_exp, n)
                if p == 0:
                    if h:
                        pe.wait_ge(s_osb, h)
                    else:
                        pe.wait_ge(s_ones, 1)
                for kt in range(2 * p, min(2 * p + 2, T0)):
                    r, q = rows(kt, N0), kt % 4
                    mm = pe.matmul(psO[32 * q:32 * q + 32, :], V[0:r, kt, h * D0:(h + 1) * D0],
                                   pt[0:r, n % NPT0, (kt % 2) * 512:(kt % 2) * 512 + 512],
                                   start=(kt < 4), stop=(kt >= T0 - 4), skip_group_check=True)
                mm.then_inc(s_pv, 1)
            elif k == "S":
                h, j = item[1], item[1] % 4
                pe.wait_ge(s_acc, 8 * (h + 1))
                for e in range(2):
                    mm = pe.matmul(psM[32 * j:32 * j + 32, :], ones[:, :], psum[:, h % 2, e * 512:e * 512 + 512],
                                   start=(e == 0), stop=(e == 1), skip_group_check=True)
                mm.then_inc(s_m, 1)
            elif k == "X":
                g = item[1]
                pe.wait_ge(s_osb, 4 * (g + 1))
                for j in range(4):
                    mm = pe.matmul(psM[32 * j:32 * j + 32, :], sel[:, 0, :], osb[:, j, :],
                                   start=True, stop=True, skip_group_check=True)
                mm.then_inc(s_m, 1)


def middle(nc, ctx, ios, b, keep, sem):
    attnT, ident = keep["attnT"], keep["ident"]
    x1, k1, q1, V1 = keep["x1"], keep["k1"], keep["q1"], keep["V1"]

    def sb(name, shape, dt=F32):
        return ctx.enter_context(nc.sbuf_tensor("mid_" + name, shape, dt))

    ctxT = keep["hT"][:, :, 0:N1]
    x, (wk1, wv1), wo = keep["tile_a"], narrow_weights(keep["tile_b"]), keep["tile_c"]
    wq1 = attnT
    ob, pw, b2, bv1 = (sb(n, [P, w]) for n, w in (("ob", D), ("pw", D), ("b2", D), ("bv1", P)))
    b1, bq, bk = keep["b1"], keep["bq1"], keep["bk1"]
    bqs = sb("bqs", [P, KO])
    w1, w2 = sb("w1", [P, 4, D]), sb("w2", [P, 4, D])
    split_w = keep["split_w"].rearrange("p (w a c n) -> p w a c n", w=2, a=2, c=2)
    w1s, w2s = split_w[:, 0], split_w[:, 1]
    xo, yn = sb("xo", [P, QT, D]), sb("yn", [P, QT, D])
    y = x1
    ssq, rs, mhalf = (sb(n, [P, QT]) for n in ("ssq", "rs", "mhalf"))
    nTs = sb("nhi", [P, KO, L], F32R), keep["qst"]
    x1T = w1
    kst, qst, qlast = key_stacks(keep["split_w"]), keep["qst"], keep["qlast"]
    hb = sb("hb", [P, 2, L])
    hs = sb("hs", [P, 2, 2, L], F32R)
    val = sb("val", [P, 2, 512])
    junk = sb("junk", [P, D])
    acc = ctx.enter_context(nc.psum_tensor("mid_acc", [P, QT, 512], F32))
    psV = ctx.enter_context(nc.psum_tensor("mid_psV", [P, 2, 512], F32))
    psS = ctx.enter_context(nc.psum_tensor("mid_psS", [P, 2, 512], F32))

    s_wkv, s_wo, s_x, s_c, s_wq1 = (sem("mid_" + n) for n in ("wkv1_in", "wo_in", "x_in", "bc_in", "wq1_in"))
    s_wo1, s_mn1, s_c1, s_last = (sem("l1_" + n) for n in ("wo_in", "maskN_in", "bc_in", "last_rows"))
    s_k1 = [sem(f"l1_k_in{i}") for i in range(2)]
    s_stack = [sem(f"l1_q_in{i}") for i in range(SLOTS)]
    s_w = [sem(f"mid_mlp_w_in{i}") for i in range(4)]
    s_v, s_vfree, s_s, s_sfree = (sem("mid_" + n) for n in ("v_full", "v_free", "s_full", "s_free"))
    s_pre, s_y, s_ssq, s_rs, s_yn = (sem("mid_" + n) for n in ("pre", "y", "ssq", "rs", "yn"))
    s_ws1, s_ws2, s_hlo, s_nlo = (sem("mid_" + n) for n in ("w1_split", "w2_split", "hidden_lo", "normed_lo"))
    s_h, s_half, s_x1, s_split, s_one = (sem("mid_" + n) for n in ("mlp_step", "minus_half", "x1", "split", "ones"))

    for_act = [("K", c) for c in range(4)] + [("T", q) for q in range(QT)] + [("H", f) for f in range(NF)] \
        + [("XT", q) for q in range(QT)] + [("Q", g) for g in range(KO)]
    for_dve = [("O", q) for q in range(QT)] + [("V", t) for t in range(T1)]
    na = {x: i + 1 for i, x in enumerate(for_act)}
    nv = {x: i + 1 for i, x in enumerate(for_dve)}
    kq = {x: i + 1 for i, x in enumerate([x for x in for_act if x[0] in ("K", "Q")])}

    block = ctx.enter_context(nc.Block())

    @block.sync
    def _(sp):
        for f in range(NF):
            if f >= 4:
                sp.wait_ge(s_ws1, 2 * (f - 3))
                sp.wait_ge(s_ws2, 2 * (f - 3))
            sp.dma_start(w1[:, f % 4, :], ios["w1"][f]).then_inc(s_w[f % 4], 16)
            sp.dma_start(w2[:, f % 4, :], ios["w2"][f]).then_inc(s_w[f % 4], 16)
            if f == 3:
                sp.wait_ge(s_v, QT)
                sp.dma_start(wq1[:, :, :], ios["wq1"]).then_inc(s_wq1, 16)
            if f == 5:
                sp.wait_ge(s_v, QT + T1)
                sp.dma_start(wo[:, :, :], ios["wo1"]).then_inc(s_wo1, 16)
                for q in range(QT):
                    sp.dma_start(keep["hT"][:, q, 0:N1], ios["maskN"][b, q]).then_inc(s_mn1, 16)
        sp.wait_ge(s_pre, 5 + QT)
        for i, name in enumerate(("bo1", "gamma", "beta")):
            sp.dma_start(x[:, i, :], ios[name].partition_broadcast(P)).then_inc(s_c1, 16)
        sp.wait_ge(s_h, NF)
        for kv in range(2):
            copy_keys(sp, kst, k1, kv, s_k1)
        sp.wait_ge(s_last, 7)
        sp.wait_ge(s_split, kq[("Q", 0)])
        for h in range(SLOTS):
            copy_queries(sp, qst, q1, qlast, h, s_stack)

    @block.gpsimd
    def _(pool):
        pool.memset(V1[:, :, :, D1:2 * D1], 1.0).then_inc(s_one, 1)
        pool.memset(mhalf[:, :], -0.5).then_inc(s_half, 1)
        for item in for_act:
            if item[0] not in ("K", "Q"):
                continue
            n = kq[item]
            if item[0] == "K":
                lo, hi = PR0[item[1]], PR0[item[1] + 1]
                dst = [k1[:, i, lo:hi] for i in (0, 1)]
            else:
                lo, hi = 0, L
                dst = [q1[:, item[1], i, :] for i in (0, 1)]
            v = val[:, n % 2, 0:hi - lo]
            pool.wait_ge(s_sfree, na[item])
            pool.tensor_tensor(dst[1], v, dst[0].bitcast(F32), ALU.subtract).then_inc(s_split, 1)
            if item == ("K", 3):
                pool.wait_ge(s_half, 1)
                pool.wait_ge(s_rs, 1)
                pool.tensor_tensor(rs[:, :], rs[:, :], mhalf[:, :], ALU.pow).then_inc(s_rs, 1)

    @block.scalar
    def _(act):
        for dst, name in ((ob, "ob0"), (pw, "pw0"), (b2, "b2"), (bv1, "bv1")):
            act.dma_start(dst[:, :], ios[name].partition_broadcast(P)).then_inc(s_c, 16)
        for item in for_act:
            k, i = item
            n = na[item]
            src = psS[:, n % 2, :]
            act.wait_ge(s_s, n)
            if k in ("K", "Q"):
                m = kq[item]
                if m > 2:
                    act.wait_ge(s_split, m - 2)
                w = PR0[i + 1] - PR0[i] if k == "K" else L
                if k == "Q" and i == 0:
                    act.wait_ge(s_pre, 1)
                high = k1[:, 0, PR0[i]:PR0[i + 1]] if k == "K" else q1[:, i, 0, :]
                bias, scale = (bk[:, 0:1], 1.0) if k == "K" else (bqs[:, i:i + 1], D1 ** -0.5)
                act.activation(high, src[:, 0:w], ACT.Identity, bias=bias, scale=scale)
                act.activation(val[:, m % 2, 0:w], src[:, 0:w], ACT.Identity, bias=bias, scale=scale)\
                   .then_inc(s_sfree, 1)
            elif k == "H":
                if i >= 2:
                    act.wait_ge(s_h, i - 1)
                    act.wait_ge(s_hlo, i - 1)
                act.activation(hs[:, i % 2, 0, :], src, ACT.Gelu_apprx_tanh, bias=b1[:, i:i + 1])
                act.activation(hb[:, i % 2, :], src, ACT.Gelu_apprx_tanh, bias=b1[:, i:i + 1]).then_inc(s_sfree, 1)
            else:
                dst = nTs[0] if k == "T" else x1T
                act.activation(dst[:, :, i * P:(i + 1) * P], src.rearrange("p (k n) -> p k n", k=KO),
                               ACT.Copy).then_inc(s_sfree, 1)

    @block.vector
    def _(dve):
        dve.tensor_scalar(bqs[:, :], bq[:, :], D1 ** -0.5, None, ALU.mult).then_inc(s_pre, 1)
        dve.wait_ge(s_x, 16)
        dve.wait_ge(s_c, 64)
        for q in range(QT):
            dve.tensor_tensor(xo[:, q, :], x[:, q, :], ob[:, :], ALU.add).then_inc(s_pre, 1)
        def values(t):
            n, r = nv[("V", t)], rows(t, N1)
            dve.wait_ge(s_v, n)
            dve.tensor_tensor(V1[0:r, t, :, 0:D1],
                              psV[0:r, n % 2, 0:P].rearrange("p (k d) -> p k d", d=D1),
                              bv1[0:r, :].rearrange("p (k d) -> p k d", d=D1), ALU.add).then_inc(s_vfree, 1)

        def split(w, ws, s_ws, f):
            dve.wait_ge(s_w[f % 4], 32 * (f // 4 + 1))
            dve.tensor_copy(ws[:, f % 2, 0, :], w[:, f % 4, :]).then_inc(s_ws, 1)
            dve.wait_ge(s_ws, 2 * f + 1)
            dve.tensor_tensor(ws[:, f % 2, 1, :], w[:, f % 4, :], ws[:, f % 2, 0, :].bitcast(F32), ALU.subtract)\
               .then_inc(s_ws, 1)

        split(w1, w1s, s_ws1, 0)
        split(w1, w1s, s_ws1, 1)
        split(w2, w2s, s_ws2, 0)
        for q in range(QT):
            n = nv[("O", q)]
            dve.wait_ge(s_v, n)
            dve.wait_ge(s_pre, 2 + q)
            dve.tensor_tensor(y[:, q, :], psV[:, n % 2, :], xo[:, q, :], ALU.add).then_inc(s_y, 1)
            dve.wait_ge(s_y, q + 1)
            if q:
                dve.wait_ge(s_ssq, q)
            dve.tensor_tensor_reduce(junk[:, :], y[:, q, :], y[:, q, :], 1.0 / D, 0.0, ALU.mult, ALU.add,
                                     ssq[:, q:q + 1]).then_inc(s_ssq, 1)
        dve.wait_ge(s_ssq, QT)
        dve.tensor_scalar(rs[:, :], ssq[:, :], EPS, None, ALU.add).then_inc(s_rs, 1)
        values(0)
        values(1)
        dve.wait_ge(s_rs, 2)
        for q in range(QT):
            dve.scalar_tensor_tensor(out=yn[:, q, :], in0=y[:, q, :], scalar=rs[:, q:q + 1], in1=pw[:, :],
                                     op0=ALU.mult, op1=ALU.mult).then_inc(s_yn, 1)

        for t in range(2, T1):
            values(t)
        for q in range(QT):
            n = na[("T", q)]
            dve.wait_ge(s_sfree, n)
            dve.tensor_tensor(nTs[1][:, :, q * P:(q + 1) * P], psS[:, n % 2, :].rearrange("p (k n) -> p k n", k=KO),
                              nTs[0][:, :, q * P:(q + 1) * P].bitcast(F32), ALU.subtract).then_inc(s_nlo, 1)
        for q in range(QT):
            dve.tensor_tensor(xo[:, q, :], x[:, q, :], b2[:, :], ALU.add).then_inc(s_pre, 1)
        for f in range(NF):
            dve.wait_ge(s_sfree, na[("H", f)])
            dve.tensor_tensor(hs[:, f % 2, 1, :], hb[:, f % 2, :], hs[:, f % 2, 0, :].bitcast(F32), ALU.subtract)\
               .then_inc(s_hlo, 1)
            if f + 2 < NF:
                dve.wait_ge(s_s, na[("H", f)])
                split(w1, w1s, s_ws1, f + 2)
            if f + 1 < NF:
                if f:
                    dve.wait_ge(s_h, f)
                split(w2, w2s, s_ws2, f + 1)
        dve.wait_ge(s_h, NF)
        for q in range(QT):
            dve.wait_ge(s_pre, 6 + q)
            dve.tensor_tensor(x1[:, q, :], acc[:, q, :], xo[:, q, :], ALU.add).then_inc(s_x1, 1)
        dve.memset(qlast[64:128, :].bitcast(F32), 0.0).then_inc(s_last, 1)
        for i in range(2):
            dve.memset(kst[64:128, i, :].bitcast(F32), 0.0).then_inc(s_last, 1)
            dve.memset(kst[0:64, i, N1:N1 + 1].bitcast(F32), 0.0).then_inc(s_last, 1)
        dve.wait_ge(s_last, 5)
        for i in range(2):
            dve.memset(kst[96:98, i, :].bitcast(F32), 1.0).then_inc(s_last, 1)

    @block.tensor
    def _(pe):
        def bank_s(item):
            n = na[item]
            if n > 2:
                pe.wait_ge(s_sfree, n - 2)
                if for_act[n - 3][0] == "T":
                    pe.wait_ge(s_nlo, for_act[n - 3][1] + 1)
            return psS[:, n % 2, :]

        def bank_v(item):
            n = nv[item]
            if 2 < n <= QT + 2:
                pe.wait_ge(s_y, n - 2)
            elif n > QT + 2:
                pe.wait_ge(s_vfree, n - 2 - QT)
            return psV[:, n % 2, :]

        pe.wait_ge(s_wkv, 32)
        for c in range(4):
            dst, lo, hi = bank_s(("K", c)), PR0[c], PR0[c + 1]
            for ko in range(KO):
                mm = pe.matmul(dst[:, 0:hi - lo], wk1[:, ko, :], ctxT[:, ko, lo:hi], start=(ko == 0), stop=(ko == KO - 1))
            mm.then_inc(s_s, 1)
        pe.wait_ge(s_wo, 16)
        for q in range(QT):
            dst = bank_v(("O", q))
            for ko in range(KO):
                mm = pe.matmul(dst, attnT[:, ko, q * P:(q + 1) * P], wo[:, ko, :], start=(ko == 0), stop=(ko == KO - 1))
            mm.then_inc(s_v, 1)
        for t in range(T1):
            dst, r = bank_v(("V", t)), rows(t, N1)
            for ko in range(KO):
                mm = pe.matmul(dst[0:r, 0:P], ctxT[:, ko, t * P:t * P + r], wv1[:, ko, :], start=(ko == 0), stop=(ko == KO - 1))
            mm.then_inc(s_v, 1)
        for q in range(QT):
            dst = bank_s(("T", q))
            pe.wait_ge(s_yn, q + 1)
            for ko in range(KO):
                mm = pe.transpose(dst[:, ko * P:(ko + 1) * P], yn[:, q, ko * P:(ko + 1) * P], ident[:, :])
            mm.then_inc(s_s, 1)

        def down(f):
            pe.wait_ge(s_hlo, f + 1)
            pe.wait_ge(s_ws2, 2 * (f + 1))
            for q in range(QT):
                for a, c in SPLIT:
                    mm = pe.matmul(acc[:, q, :], hs[:, f % 2, a, q * P:(q + 1) * P], w2s[:, f % 2, c, :],
                                   start=(f == 0 and a == c), stop=(f == NF - 1 and (a, c) == SPLIT[-1]))
            mm.then_inc(s_h, 1)

        pe.wait_ge(s_nlo, QT)
        for f in range(NF):
            dst = bank_s(("H", f))
            pe.wait_ge(s_ws1, 2 * (f + 1))
            for ko in range(KO):
                for a, c in SPLIT:
                    mm = pe.matmul(dst, w1s[:, f % 2, a, ko * P:(ko + 1) * P], nTs[c][:, ko, :],
                                   start=(ko == 0 and a == c), stop=(ko == KO - 1 and (a, c) == SPLIT[-1]))
            mm.then_inc(s_s, 1)
            if f:
                down(f - 1)
        down(NF - 1)
        for q in range(QT):
            dst = bank_s(("XT", q))
            pe.wait_ge(s_x1, q + 1)
            for ko in range(KO):
                mm = pe.transpose(dst[:, ko * P:(ko + 1) * P], x1[:, q, ko * P:(ko + 1) * P], ident[:, :])
            mm.then_inc(s_s, 1)
        pe.wait_ge(s_sfree, na[("XT", QT - 1)])
        pe.wait_ge(s_wq1, 16)
        for g in range(KO):
            dst = bank_s(("Q", g))
            for ko in range(KO):
                mm = pe.matmul(dst, wq1[:, ko, g * P:(g + 1) * P], x1T[:, ko, :], start=(ko == 0), stop=(ko == KO - 1))
            mm.then_inc(s_s, 1)


def key_stacks(tile):
    return tile[:, 0:2 * (N1 + 1)].rearrange("p (a n) -> p a n", a=2)


def copy_keys(sp, kst, k1, kv, s_k):
    for r in range(4):
        sp.dma_start(kst[16 * r:16 * r + 16, kv % 2, 0:N1].bitcast(F32),
                     k1[16 * kv:16 * kv + 16, r % 2, :].bitcast(F32)).then_inc(s_k[kv % 2], 16)


def copy_queries(sp, qst, q1, qlast, h, s_stack):
    g, j, s = h // 8, h % 8, h % SLOTS
    for r in range(4):
        sp.dma_start(qst[16 * r:16 * r + 16, s, :].bitcast(F32),
                     q1[16 * j:16 * j + 16, g, r // 2, :].bitcast(F32)).then_inc(s_stack[s], 16)
    sp.dma_start(qst[64:128, s, :].bitcast(F32), qlast[64:128, :].bitcast(F32)).then_inc(s_stack[s], 16)


def layer1_attention(nc, ctx, ios, b, keep, sem):
    plan = plan_layer1()
    ident, sel = keep["identR"], keep["sel"]
    x1, k1, q1, V1 = keep["x1"], keep["k1"], keep["q1"], keep["V1"]

    def sb(name, shape, dt=F32):
        return ctx.enter_context(nc.sbuf_tensor("l1_" + name, shape, dt))

    def ps(name, shape):
        return ctx.enter_context(nc.psum_tensor("l1_" + name, shape, F32))

    maskN = keep["hT"][:, :, 0:N1]
    maskT = sb("maskT", [P, T1, L])
    kst = key_stacks(keep["split_w"])
    qst = keep["qst"]
    qlast = keep["qlast"]
    pt = sb("pt", [P, NPT1, 1024])
    osb = sb("osb", [P, 8, L])
    rsum, junk = keep["tile_b"][:, 0, :], keep["tile_b"][:, 1:3, 0:402]
    acc = sb("acc", [P, 2, QT, 4])
    nmax = sb("nmax", [P, 2, QT])
    mz = sb("mz", [P, 2, QT, 98], F32R)
    attn, wo = keep["attnT"], keep["tile_c"]
    bo, gam, bet = (keep["tile_a"][:, i, :] for i in range(3))
    st = sb("st", [P, QT, 6])
    mv = sb("mv", [P, QT, 2])
    rstd, mhalf = sb("rstd", [P, QT]), sb("mhalf", [P, 1])
    psR = ps("psR", [P, NR, 512])
    psB, psO = ps("psB", [P, 4, 512]), ps("psO", [P, 512])

    s_mn, s_mt, s_wo, s_c = (sem("l1_" + n) for n in ("maskN_in", "maskT_in", "wo_in", "bc_in"))
    s_k = [sem(f"l1_k_in{i}") for i in range(2)]
    s_stack = [sem(f"l1_q_in{i}") for i in range(SLOTS)]
    s_last = sem("l1_last_rows")
    s_m = sem("l1_m_full")
    s_a, s_red = sem("l1_a_full"), sem("l1_a_reduced")
    s_nm, s_mh, s_ml = sem("l1_nmax"), sem("l1_max_hi"), sem("l1_max_hilo")
    s_b, s_add, s_exp, s_pv = sem("l1_b_full"), sem("l1_masked"), sem("l1_exp"), sem("l1_pv")
    s_copy, s_padd, s_zero = sem("l1_copied"), sem("l1_masked_by_pool"), sem("l1_zeros")
    s_osb, s_rs, s_att, s_rows = sem("l1_osb"), sem("l1_rsum"), sem("l1_att"), sem("l1_max_rows")
    s_var, s_rstd, s_half = sem("l1_var"), sem("l1_rstd"), sem("l1_minus_half")
    s_o, s_y, s_z, s_out = sem("l1_o_full"), sem("l1_y"), sem("l1_norm"), sem("l1_out")

    ring = order(plan, "A", "M", "Y", "X")
    in_ring = [x for x in plan if x in ring]
    m_uses = order(plan, "M", "Y", "X")
    aa = order(plan, "A")
    bb = order(plan, "B")
    by_pool = order([x for x in plan if x[0] == "B" and x[2] in POOL_PAIRS], "B")
    by_dve = order([x for x in plan if x[0] == "B" and x[2] not in POOL_PAIRS], "B")

    block = ctx.enter_context(nc.Block())

    @block.sync
    def _(sp):
        for t in range(T1):
            r = rows(t, N1)
            sp.dma_start(maskT[0:r, t, :], ios["maskT"][b, t * P:t * P + r, :]).then_inc(s_mt, 16)
        for h in range(SLOTS, H1):
            kv = h // GQ
            if h % GQ == 0 and kv >= 2:
                sp.wait_ge(s_b, bb[("B", GQ * (kv - 1) - 1, PAIRS1 - 1)])
                copy_keys(sp, kst, k1, kv, s_k)
            sp.wait_ge(s_b, bb[("B", h - SLOTS, PAIRS1 - 1)])
            copy_queries(sp, qst, q1, qlast, h, s_stack)
        for q in range(QT):
            sp.wait_ge(s_z, q + 1)
            sp.dma_start(ios["out"][b, q], x1[:, q, :]).then_inc(s_out, 16)
        sp.wait_ge(s_out, 16 * QT)

    @block.gpsimd
    def _(pool):
        pool.memset(mhalf[:, :], -0.5).then_inc(s_half, 1)
        pool.memset(mz[:, :, :, 0:96].bitcast(F32), 0.0).then_inc(s_zero, 1)
        pool.wait_ge(s_mt, 16 * T1)
        for item in by_pool:
            n, kt = bb[item], 2 * item[2]
            pool.wait_ge(s_copy, by_pool[item])
            tile = pt[:, n % NPT1, :]
            pool.tensor_tensor(tile, tile, maskT[:, kt:kt + 2, :].rearrange("p a n -> p (a n)"), ALU.add)\
                .then_inc(s_padd, 1)
        for q in range(QT):
            pool.wait_ge(s_var, q + 1)
            pool.tensor_tensor(rstd[:, q:q + 1], rstd[:, q:q + 1], mhalf[:, :], ALU.pow).then_inc(s_rstd, 1)

    @block.scalar
    def _(act):
        for item in plan:
            if item[0] == "M":
                psM = psR[:, ring[item] % NR, :]
                act.wait_ge(s_m, m_uses[item])
                act.activation(qst[96:98, item[1] % SLOTS, :], psM[96:98, :], ACT.Copy).then_inc(s_rows, 1)
            elif item[0] == "B" and item in by_pool:
                n = bb[item]
                act.wait_ge(s_b, n)
                if n > NPT1:
                    act.wait_ge(s_pv, n - NPT1)
                act.activation(pt[:, n % NPT1, :], psB[:, 2 * (n % 2):2 * (n % 2) + 2, :].rearrange("p a n -> p (a n)"),
                               ACT.Copy).then_inc(s_copy, 1)
            elif item[0] == "P":
                at = ("B", *item[1:])
                n, kt = bb[at], 2 * item[2]
                r, w = (P, 1024) if kt + 1 < T1 else (rows(kt, N1), 512)
                if at in by_pool:
                    act.wait_ge(s_padd, by_pool[at])
                else:
                    act.wait_ge(s_add, by_dve[at])
                act.activation(pt[0:r, n % NPT1, 0:w], pt[0:r, n % NPT1, 0:w], ACT.Exp).then_inc(s_exp, 1)
            elif item[0] == "E":
                h = item[1]
                act.wait_ge(s_pv, PAIRS1 * (h + 1))
                if h >= 8:
                    act.wait_ge(s_m, m_uses[("X", h // 8 - 1)])
                act.activation(osb[:, h % 8, :], psO[:, :], ACT.Copy).then_inc(s_osb, 1)

    @block.vector
    def _(dve):
        dve.wait_ge(s_mn, 16 * QT)
        for item in plan:
            if item[0] == "A":
                _, h, qt, c = item
                n, lo, hi = aa[item], CH1[c], min(CH1[c + 1], N1)
                dve.wait_ge(s_a, n)
                if h >= 2 and qt == c == 0:
                    dve.wait_ge(s_nm, h - 1)
                if n > 2:
                    dve.wait_ge(s_red, n - 2)
                dve.tensor_tensor_reduce(junk[:, n % 2, 0:hi - lo], psR[:, ring[item] % NR, 0:hi - lo], maskN[:, qt, lo:hi],
                                         1.0, -3e38, ALU.add, ALU.max, acc[:, h % 2, qt, c:c + 1]).then_inc(s_red, 1)
            elif item[0] == "N":
                h = item[1]
                dve.wait_ge(s_red, 16 * (h + 1))
                dve.tensor_reduce(nmax[:, h % 2, :], acc[:, h % 2, :, :], AX.X, ALU.max, negate=True).then_inc(s_nm, 1)
            elif item[0] == "H":
                h = item[1]
                dve.wait_ge(s_nm, h + 1)
                if h >= 2:
                    dve.wait_ge(s_m, m_uses[("M", h - 2)])
                dve.tensor_copy(mz[:, h % 2, :, 96], nmax[:, h % 2, :]).then_inc(s_mh, 1)
            elif item[0] == "L":
                h = item[1]
                dve.wait_ge(s_mh, h + 1)
                dve.tensor_tensor(mz[:, h % 2, :, 97], nmax[:, h % 2, :], mz[:, h % 2, :, 96].bitcast(F32),
                                  ALU.subtract).then_inc(s_ml, 1)
            elif item[0] == "B" and item in by_dve:
                n, kt = bb[item], 2 * item[2]
                r, w = (P, 1024) if kt + 1 < T1 else (rows(kt, N1), 512)
                if by_dve[item] == 1:
                    dve.wait_ge(s_mt, 16 * T1)
                dve.wait_ge(s_b, n)
                if n > NPT1:
                    dve.wait_ge(s_pv, n - NPT1)
                dve.tensor_tensor(pt[0:r, n % NPT1, 0:w],
                                  psB[0:r, 2 * (n % 2):2 * (n % 2) + 2, :].rearrange("p a n -> p (a n)")[:, 0:w],
                                  maskT[0:r, kt:kt + w // 512, :].rearrange("p a n -> p (a n)"),
                                  ALU.add).then_inc(s_add, 1)
            elif item[0] == "Y":
                psM = psR[:, ring[item] % NR, :]
                dve.wait_ge(s_m, m_uses[item])
                if item[1]:
                    dve.wait_ge(s_att, item[1])
                dve.reciprocal(rsum[:, :], psM).then_inc(s_rs, 1)
            elif item[0] == "X":
                psM = psR[:, ring[item] % NR, :]
                dve.wait_ge(s_m, m_uses[item])
                dve.wait_ge(s_rs, item[1] + 1)
                dve.tensor_tensor(attn[:, item[1], :], psM, rsum[:, :], ALU.mult).then_inc(s_att, 1)
        dve.wait_ge(s_c, 48)
        for q in range(QT):
            dve.tensor_tensor(x1[:, q, :], x1[:, q, :], bo, ALU.add).then_inc(s_y, 1)
        for q in range(QT):
            dve.wait_ge(s_o, q + 1)
            dve.wait_ge(s_y, 4 + 4 * q)
            dve.tensor_tensor(x1[:, q, :], psB[:, q, :], x1[:, q, :], ALU.add).then_inc(s_y, 1)
            dve.wait_ge(s_y, 5 + 4 * q)
            dve.bn_stats(st[:, q, :], x1[:, q, :]).then_inc(s_y, 1)
            dve.wait_ge(s_y, 6 + 4 * q)
            dve.bn_aggr(mv[:, q, :], st[:, q, :]).then_inc(s_y, 1)
            dve.wait_ge(s_y, 7 + 4 * q)
            dve.tensor_scalar(rstd[:, q:q + 1], mv[:, q, 1:2], EPS, None, ALU.add).then_inc(s_var, 1)
            dve.scalar_tensor_tensor(out=x1[:, q, :], in0=x1[:, q, :], scalar=mv[:, q, 0:1], in1=gam,
                                     op0=ALU.subtract, op1=ALU.mult).then_inc(s_y, 1)
        for q in range(QT):
            dve.wait_ge(s_rstd, q + 1)
            dve.wait_ge(s_y, 8 + 4 * q)
            dve.scalar_tensor_tensor(out=x1[:, q, :], in0=x1[:, q, :], scalar=rstd[:, q:q + 1], in1=bet,
                                     op0=ALU.mult, op1=ALU.add).then_inc(s_z, 1)

    @block.tensor
    def _(pe):
        for item in plan:
            k = item[0]
            if item in ring:
                psM = psR[:, ring[item] % NR, :]
                if ring[item] > NR:
                    last = in_ring[ring[item] - NR - 1]
                    pe.wait_ge({"A": s_red, "M": s_rows, "Y": s_rs, "X": s_att}[last[0]],
                               aa[last] if last in aa else last[1] + 1)
            if k == "A":
                _, h, qt, c = item
                n, s, kv = aa[item], h % SLOTS, h // GQ
                if qt == c == 0:
                    pe.wait_ge(s_last, 7)
                    pe.wait_ge(s_stack[s], 80 * (h // SLOTS + 1))
                    pe.wait_ge(s_k[kv % 2], 64 * (kv // 2 + 1))
                pe.matmul(psM[:, 0:CH1[c + 1] - CH1[c]], qst[:, s, qt * P:(qt + 1) * P],
                          kst[:, kv % 2, CH1[c]:CH1[c + 1]], start=True, stop=True).then_inc(s_a, 1)
            elif k == "M":
                h = item[1]
                pe.wait_ge(s_ml, h + 1)
                if h == 0:
                    pe.wait_ge(s_zero, 1)
                for qt in range(QT):
                    mm = pe.matmul(psM[0:98, qt * P:(qt + 1) * P], mz[:, h % 2, qt, :], ident[:, :],
                                   start=True, stop=True)
                mm.then_inc(s_m, 1)
            elif k == "B":
                _, h, p = item
                n, s, kv = bb[item], h % SLOTS, h // GQ
                if p == 0:
                    pe.wait_ge(s_rows, h + 1)
                if n > 2:
                    before = ("B", *divmod(n - 3, PAIRS1))
                    pe.wait_ge(s_copy if before in by_pool else s_add, (by_pool if before in by_pool else by_dve)[before])
                for kt in range(2 * p, min(2 * p + 2, T1)):
                    r = rows(kt, N1)
                    mm = pe.matmul(psB[0:r, 2 * (n % 2) + kt % 2, :], kst[:, kv % 2, kt * P:kt * P + r], qst[:, s, :],
                                   start=True, stop=True)
                mm.then_inc(s_b, 1)
            elif k == "W":
                _, h, p = item
                n, kv = bb[("B", h, p)], h // GQ
                pe.wait_ge(s_exp, n)
                if p == 0 and h:
                    pe.wait_ge(s_osb, h)
                for kt in range(2 * p, min(2 * p + 2, T1)):
                    r, q = rows(kt, N1), kt % 4
                    mm = pe.matmul(psO[32 * q:32 * q + 32, :], V1[0:r, kt, kv, :],
                                   pt[0:r, n % NPT1, (kt % 2) * 512:(kt % 2) * 512 + 512],
                                   start=(kt < 4), stop=(kt >= T1 - 4), skip_group_check=True)
                mm.then_inc(s_pv, 1)
            elif k == "O":
                pe.wait_ge(s_wo, 16)
                pe.wait_ge(s_att, KO - 1)
                pe.wait_ge(s_copy, len(by_pool))
                pe.wait_ge(s_add, len(by_dve))
                for q in range(QT):
                    for ko in range(KO - 1):
                        pe.matmul(psB[:, q, :], attn[:, ko, q * P:(q + 1) * P], wo[:, ko, :], start=(ko == 0), stop=False)
            elif k in ("Y", "X"):
                g = item[1]
                pe.wait_ge(s_osb, 8 * (g + 1))
                for j in range(8):
                    mm = pe.matmul(psM[32 * (j // 2):32 * (j // 2) + 32, :], sel[:, 1 + 2 * (k == "Y") + j % 2, :],
                                   osb[:, j, :], start=(j % 2 == 0), stop=(j % 2 == 1), skip_group_check=True)
                mm.then_inc(s_m, 1)
        pe.wait_ge(s_att, KO)
        for q in range(QT):
            pe.matmul(psB[:, q, :], attn[:, KO - 1, q * P:(q + 1) * P], wo[:, KO - 1, :], start=False, stop=True)\
              .then_inc(s_o, 1)


def two_layers(nc, ios):
    sems = {}

    def sem(name):
        if name not in sems:
            sems[name] = nc.alloc_semaphore(name)
        return sems[name]

    with ExitStack() as outer:
        def sb(stack, name, shape, dt=F32):
            return stack.enter_context(nc.sbuf_tensor(name, shape, dt))

        keep = {"ident": sb(outer, "ident", [P, P]), "sel": sb(outer, "sel", [P, 5, 32]),
                "identR": sb(outer, "identR", [P, P], F32R), "attnT": sb(outer, "attnT", [P, KO, L]),
                "hT": sb(outer, "hT", [P, KO, N0]),
                **{n: sb(outer, n, [P, w]) for n, w in (("b1", NF), ("bq1", KO), ("bk1", 1))},
                **{n: sb(outer, n, [P, KO, D]) for n in ("tile_a", "tile_b", "tile_c")}}
        loaded = nc.alloc_semaphore("consts_in")
        with nc.Block() as block:
            @block.sync
            def _(sp):
                sp.dma_start(keep["ident"][:, :], ios["ident"]).then_inc(loaded, 16)
                sp.dma_start(keep["sel"][:, :, :], ios["sel"]).then_inc(loaded, 16)
                for name in ("b1", "bq1", "bk1"):
                    sp.dma_start(keep[name][:, :], ios[name]).then_inc(loaded, 16)
                sp.wait_ge(loaded, 80)

            @block.vector
            def _(dve):
                dve.wait_ge(loaded, 80)
                dve.tensor_copy(keep["identR"][:, :], keep["ident"][:, :])
        with nc.Fori(0, B) as b:
            with ExitStack() as ctx:
                layer0_attention(nc, ctx, ios, b, keep, sem)
            with ExitStack() as inner:
                keep["x1"] = sb(inner, "x1", [P, QT, D])
                keep["k1"] = sb(inner, "k1", [P, 2, N1], F32R)
                keep["q1"] = sb(inner, "q1", [P, KO, 2, L], F32R)
                keep["split_w"] = sb(inner, "split_w", [P, 8 * D], F32R)
                keep["qst"] = sb(inner, "qst", [P, SLOTS, L], F32R)
                keep["qlast"] = sb(inner, "qlast", [P, L], F32R)
                keep["V1"] = sb(inner, "V1", [P, T1, KV1, 2 * D1])
                with ExitStack() as ctx:
                    middle(nc, ctx, ios, b, keep, sem)
                with ExitStack() as ctx:
                    layer1_attention(nc, ctx, ios, b, keep, sem)
            for s in sems.values():
                nc.sync.sem_clear(s)
            nc.all_engine_barrier()


def layout(i):
    import numpy as np
    a = {k: np.asarray(v) for k, v in i.items()}

    def ktiles(w):
        return np.ascontiguousarray(w.reshape(KO, P, -1).transpose(1, 0, 2))

    def cols(v):
        return np.ascontiguousarray(v.reshape(-1, P).T)

    def tokT(x):
        return np.ascontiguousarray(x.transpose(0, 2, 1).reshape(B, KO, P, -1).transpose(0, 2, 1, 3))

    def row_tiles(x):
        return np.ascontiguousarray(x.reshape(B, QT, P, -1).transpose(0, 2, 1, 3))

    kvw, kvb = a["L0_xattn_kv_w"], a["L0_xattn_kv_b"]
    m = a["mask_Bx1xSxS2_ff0"]
    tcol = np.zeros((32, 4), np.float32)
    tcol[2, 0] = 1
    tcol[0:2, 1] = 1
    tcol[2, 2] = 1
    sel = np.zeros((P, 5, 32), np.float32)
    for p in range(P):
        sel[p, 0, p % 32] = 1
    for q in range(4):
        for d in range(D1):
            for odd in range(2):
                sel[32 * q + d, 1 + odd, D1 * odd + d] = 1
                sel[32 * q + D1 + d, 3 + odd, D1 * odd + d] = 1
    return {
        "x": row_tiles(a["x"]), "xT": tokT(a["x"]), "ctxT": tokT(a["ctx_2048"]),
        "mask": np.ascontiguousarray(a["mask_BxS2_ik0"]),
        "maskN": np.ascontiguousarray(m.reshape(B, QT, P, S)),
        "maskT": np.ascontiguousarray(m.reshape(B, L, S).transpose(0, 2, 1)),
        "wq0": ktiles(a["L0_xattn_q_w"]), "wk0": ktiles(kvw[:, 0::2]), "wv0": ktiles(kvw[:, 1::2]),
        "bq0": cols(a["L0_xattn_q_b"]), "bk0": cols(kvb[0::2]), "bv0": np.ascontiguousarray(kvb[1::2]),
        "wo0": ktiles(a["L0_xattn_out_w"]), "ob0": a["L0_xattn_out_b"], "pw0": a["L0_xattn_postnorm_w"],
        "w1": np.ascontiguousarray(a["L0_xattn_mlp_w1"].reshape(KO, P, NF, P).transpose(2, 1, 0, 3).reshape(NF, P, D)),
        "b1": cols(a["L0_xattn_mlp_b1"]), "w2": np.ascontiguousarray(a["L0_xattn_mlp_w2"].reshape(NF, P, D)),
        "b2": a["L0_xattn_mlp_b2"],
        "wq1": ktiles(a["L1_xattn_Wq"]), "wk1": ktiles(a["L1_xattn_Wk"]), "wv1": ktiles(a["L1_xattn_Wv"]),
        "wo1": ktiles(a["L1_xattn_Wo"]), "bq1": cols(a["L1_xattn_bq"]), "bk1": cols(a["L1_xattn_bk"]),
        "bv1": a["L1_xattn_bv"], "bo1": a["L1_xattn_bo"], "gamma": a["L1_xattn_gamma"], "beta": a["L1_xattn_beta"],
        "tcol": tcol, "sel": sel, "ident": np.eye(P, dtype=np.float32),
    }


def kernel(**inputs):
    import concourse.bacc as bacc
    from concourse.bass_utils import run_bass_kernel_spmd
    arrays = layout(inputs)
    nc = bacc.Bacc("TRN2", target_bir_lowering=False, num_devices=1)
    ios = {n: nc.dram_tensor("in_" + n, a.shape, mybir.dt.from_np(a.dtype), kind="ExternalInput").ap()
           for n, a in arrays.items()}
    ios["out"] = nc.dram_tensor("out", (B, QT, P, D), F32, kind="ExternalOutput").ap()
    two_layers(nc, ios)
    result = run_bass_kernel_spmd(nc, [{"in_" + n: a for n, a in arrays.items()}], core_ids=[0])
    return result.results[0]["out"].reshape(B, L, D)
```
